# Optimizing a Trainium2 kernel written in Bass

```python
import numpy as np
import jax
import jax.numpy as jnp

def _softmax(x, axis=-1):
    return jax.nn.softmax(x, axis=axis)

def _gelu(x):
    return jax.nn.gelu(x, approximate=True)

def _silu(x):
    return jax.nn.silu(x)

def _sigmoid(x):
    return jax.nn.sigmoid(x)

def _layernorm(x, axis=-1, eps=1e-05):
    m = jnp.mean(x, axis=axis, keepdims=True)
    v = jnp.var(x, axis=axis, keepdims=True)
    return (x - m) / jnp.sqrt(v + eps)

def _scatter_add(tgt, idx, src, axis=0):
    return tgt.at[idx].add(src)

def _segment_sum(src, seg, n):
    return jax.ops.segment_sum(src, seg, n)
kernel_name = 'mk_dlrm_tower_d1_rec_r8_f4bc77'

def setup_inputs(seed: int=0):
    np.random.seed(seed)
    _w = jnp.asarray

    def _rec_inputs():
        import jax
        import jax.numpy as jnp
        _tk = jax.random.key(seed)
        dense_ctx = jax.random.normal(jax.random.fold_in(_tk, 190), (512, 16), jnp.float32)
        ids = jnp.stack([jax.random.randint(jax.random.fold_in(_tk, 200 + f), (512,), 0, v, jnp.int32) for f, v in enumerate([1000, 1250, 125000, 12500, 1000, 1250, 1250, 1250, 1000, 12500, 1000, 1000, 1000, 12500, 1000, 1000, 1250, 12500, 1000, 1000, 12500, 1250, 1000, 12500, 1000, 1000, 12500])], axis=1)
        tbl_0 = 0.05 * jax.random.normal(jax.random.fold_in(_tk, 500 + 0), (1000, 128), jnp.float32)
        tbl_1 = 0.05 * jax.random.normal(jax.random.fold_in(_tk, 500 + 1), (1250, 128), jnp.float32)
        tbl_2 = 0.05 * jax.random.normal(jax.random.fold_in(_tk, 500 + 2), (125000, 128), jnp.float32)
        tbl_3 = 0.05 * jax.random.normal(jax.random.fold_in(_tk, 500 + 3), (12500, 128), jnp.float32)
        tbl_4 = 0.05 * jax.random.normal(jax.random.fold_in(_tk, 500 + 4), (1000, 128), jnp.float32)
        tbl_5 = 0.05 * jax.random.normal(jax.random.fold_in(_tk, 500 + 5), (1250, 128), jnp.float32)
        tbl_6 = 0.05 * jax.random.normal(jax.random.fold_in(_tk, 500 + 6), (1250, 128), jnp.float32)
        tbl_7 = 0.05 * jax.random.normal(jax.random.fold_in(_tk, 500 + 7), (1250, 128), jnp.float32)
        tbl_8 = 0.05 * jax.random.normal(jax.random.fold_in(_tk, 500 + 8), (1000, 128), jnp.float32)
        tbl_9 = 0.05 * jax.random.normal(jax.random.fold_in(_tk, 500 + 9), (12500, 128), jnp.float32)
        tbl_10 = 0.05 * jax.random.normal(jax.random.fold_in(_tk, 500 + 10), (1000, 128), jnp.float32)
        tbl_11 = 0.05 * jax.random.normal(jax.random.fold_in(_tk, 500 + 11), (1000, 128), jnp.float32)
        tbl_12 = 0.05 * jax.random.normal(jax.random.fold_in(_tk, 500 + 12), (1000, 128), jnp.float32)
        tbl_13 = 0.05 * jax.random.normal(jax.random.fold_in(_tk, 500 + 13), (12500, 128), jnp.float32)
        tbl_14 = 0.05 * jax.random.normal(jax.random.fold_in(_tk, 500 + 14), (1000, 128), jnp.float32)
        tbl_15 = 0.05 * jax.random.normal(jax.random.fold_in(_tk, 500 + 15), (1000, 128), jnp.float32)
        tbl_16 = 0.05 * jax.random.normal(jax.random.fold_in(_tk, 500 + 16), (1250, 128), jnp.float32)
        tbl_17 = 0.05 * jax.random.normal(jax.random.fold_in(_tk, 500 + 17), (12500, 128), jnp.float32)
        tbl_18 = 0.05 * jax.random.normal(jax.random.fold_in(_tk, 500 + 18), (1000, 128), jnp.float32)
        tbl_19 = 0.05 * jax.random.normal(jax.random.fold_in(_tk, 500 + 19), (1000, 128), jnp.float32)
        tbl_20 = 0.05 * jax.random.normal(jax.random.fold_in(_tk, 500 + 20), (12500, 128), jnp.float32)
        tbl_21 = 0.05 * jax.random.normal(jax.random.fold_in(_tk, 500 + 21), (1250, 128), jnp.float32)
        tbl_22 = 0.05 * jax.random.normal(jax.random.fold_in(_tk, 500 + 22), (1000, 128), jnp.float32)
        tbl_23 = 0.05 * jax.random.normal(jax.random.fold_in(_tk, 500 + 23), (12500, 128), jnp.float32)
        tbl_24 = 0.05 * jax.random.normal(jax.random.fold_in(_tk, 500 + 24), (1000, 128), jnp.float32)
        tbl_25 = 0.05 * jax.random.normal(jax.random.fold_in(_tk, 500 + 25), (1000, 128), jnp.float32)
        tbl_26 = 0.05 * jax.random.normal(jax.random.fold_in(_tk, 500 + 26), (12500, 128), jnp.float32)
        _rk = jax.random.fold_in(_tk, 7)
        W_top1 = 0.0521996 * jax.random.normal(jax.random.fold_in(_tk, 801), (367, 512), jnp.float32)
        W_top2 = 0.0441942 * jax.random.normal(jax.random.fold_in(_tk, 802), (512, 256), jnp.float32)
        W_top3 = 0.0625 * jax.random.normal(jax.random.fold_in(_tk, 803), (256, 1), jnp.float32)
        b_top1 = jnp.zeros((512,), jnp.float32)
        b_top2 = jnp.zeros((256,), jnp.float32)
        return (dense_ctx, ids, tbl_0, tbl_1, tbl_2, tbl_3, tbl_4, tbl_5, tbl_6, tbl_7, tbl_8, tbl_9, tbl_10, tbl_11, tbl_12, tbl_13, tbl_14, tbl_15, tbl_16, tbl_17, tbl_18, tbl_19, tbl_20, tbl_21, tbl_22, tbl_23, tbl_24, tbl_25, tbl_26, W_top1, b_top1, W_top2, b_top2, W_top3)
    dense_ctx, ids, tbl_0, tbl_1, tbl_2, tbl_3, tbl_4, tbl_5, tbl_6, tbl_7, tbl_8, tbl_9, tbl_10, tbl_11, tbl_12, tbl_13, tbl_14, tbl_15, tbl_16, tbl_17, tbl_18, tbl_19, tbl_20, tbl_21, tbl_22, tbl_23, tbl_24, tbl_25, tbl_26, W_top1, b_top1, W_top2, b_top2, W_top3 = _rec_inputs()

    def _L0_rec_setup():
        import jax, jax.numpy as jnp
        import numpy as np
        NUM_FEAS = 27
        key = jax.random.key(seed)
        inputs = jax.random.normal(key, (4096, NUM_FEAS, 128), dtype=jnp.float32)
        return {'inputs': inputs}
    _L0_rec_all = _L0_rec_setup()
    _L0_rec_in = {k: v for k, v in _L0_rec_all.items() if k in ()}
    del _L0_rec_all
    return {'dense_ctx': dense_ctx, 'ids': ids, 'tbl_0': tbl_0, 'tbl_1': tbl_1, 'tbl_2': tbl_2, 'tbl_3': tbl_3, 'tbl_4': tbl_4, 'tbl_5': tbl_5, 'tbl_6': tbl_6, 'tbl_7': tbl_7, 'tbl_8': tbl_8, 'tbl_9': tbl_9, 'tbl_10': tbl_10, 'tbl_11': tbl_11, 'tbl_12': tbl_12, 'tbl_13': tbl_13, 'tbl_14': tbl_14, 'tbl_15': tbl_15, 'tbl_16': tbl_16, 'tbl_17': tbl_17, 'tbl_18': tbl_18, 'tbl_19': tbl_19, 'tbl_20': tbl_20, 'tbl_21': tbl_21, 'tbl_22': tbl_22, 'tbl_23': tbl_23, 'tbl_24': tbl_24, 'tbl_25': tbl_25, 'tbl_26': tbl_26, 'W_top1': W_top1, 'b_top1': b_top1, 'W_top2': W_top2, 'b_top2': b_top2, 'W_top3': W_top3}

def reference(dense_ctx, ids, tbl_0, tbl_1, tbl_2, tbl_3, tbl_4, tbl_5, tbl_6, tbl_7, tbl_8, tbl_9, tbl_10, tbl_11, tbl_12, tbl_13, tbl_14, tbl_15, tbl_16, tbl_17, tbl_18, tbl_19, tbl_20, tbl_21, tbl_22, tbl_23, tbl_24, tbl_25, tbl_26, W_top1, b_top1, W_top2, b_top2, W_top3):
    import jax
    import jax.numpy as jnp

    def _L0_rec_ref(inputs):
        import jax, jax.numpy as jnp
        import numpy as np
        NUM_FEAS = 27
        n = inputs.shape[1]
        dot = jnp.einsum('bnd,bmd->bnm', inputs, inputs)
        iu, ju = jnp.triu_indices(n, k=1)
        return dot[:, iu, ju]
    e = jnp.stack([tbl_0[ids[:, 0]], tbl_1[ids[:, 1]], tbl_2[ids[:, 2]], tbl_3[ids[:, 3]], tbl_4[ids[:, 4]], tbl_5[ids[:, 5]], tbl_6[ids[:, 6]], tbl_7[ids[:, 7]], tbl_8[ids[:, 8]], tbl_9[ids[:, 9]], tbl_10[ids[:, 10]], tbl_11[ids[:, 11]], tbl_12[ids[:, 12]], tbl_13[ids[:, 13]], tbl_14[ids[:, 14]], tbl_15[ids[:, 15]], tbl_16[ids[:, 16]], tbl_17[ids[:, 17]], tbl_18[ids[:, 18]], tbl_19[ids[:, 19]], tbl_20[ids[:, 20]], tbl_21[ids[:, 21]], tbl_22[ids[:, 22]], tbl_23[ids[:, 23]], tbl_24[ids[:, 24]], tbl_25[ids[:, 25]], tbl_26[ids[:, 26]]], axis=1)
    z = _L0_rec_ref(e)
    z = z.reshape(z.shape[0], -1)
    h = jnp.concatenate([z, dense_ctx], axis=1)
    h = jnp.maximum(h @ W_top1 + b_top1, 0.0)
    h = jnp.maximum(h @ W_top2 + b_top2, 0.0)
    y = h @ W_top3
    return y

_drawn_inputs = setup_inputs


def setup_inputs(seed=0):
    import zlib

    import numpy as np

    out = dict(_drawn_inputs(seed))
    spreads = {'b_top1': (0.0, 0.1), 'b_top2': (0.0, 0.1)}
    factors = {}
    for name, (base, spread) in spreads.items():
        noise = np.random.default_rng([zlib.crc32(name.encode()), seed]).standard_normal(out[name].shape)
        drawn = base * np.exp(spread * noise) if base else spread * noise
        out[name] = jnp.asarray(drawn.astype(out[name].dtype))
    for name, factor in factors.items():
        out[name] = (out[name] * factor).astype(out[name].dtype)
    return out
```

```python
from contextlib import ExitStack

import concourse.bass as bass
from concourse import mybir

NF = 27
P = 128


def dlrm_tower(nc, dense_ctx, ids, tables, w_top1, b_top1, w_top2, b_top2, w_top3, out):
    fp32 = mybir.dt.float32
    u32 = mybir.dt.uint32
    ACT = mybir.ActivationFunctionType
    ALU = mybir.AluOpType

    B, ND = dense_ctx.shape
    D = tables[0].shape[1]
    H1, H2 = w_top1.shape[1], w_top2.shape[1]
    CH = B // P
    PAD = 32
    NS = P // PAD
    NG = P // NS
    STEP = 8
    NSTEP = NG // STEP
    QF = 4
    BATCHES = [range(f, min(f + QF, NF)) for f in range(0, NF, QF)]
    NB = len(BATCHES)
    NK = (NF - 1) // 2
    PITCH = NF + NK
    KC = 3
    NR = NF // KC
    NP = NR * NK
    SPARE = P - NP
    DENSE = [range(0, SPARE), range(SPARE, ND), range(ND, ND)]
    KROWS = [NP + len(r) for r in DENSE]
    O1, O2 = H1 // P, H2 // P

    def pair_row(n, m):
        return n * NF - n * (n + 1) // 2 + (m - n - 1)

    def w1_pieces():
        for n in range(NF - 1):
            count = min(NK, NF - 1 - n)
            yield pair_row(n, n + 1), count, n // NR, NK * (n % NR), 1
        for m in range(NK):
            for c in range(KC):
                lo, hi = max(m + NF - NK, c * NR), min(NF, (c + 1) * NR)
                if lo < hi:
                    k = m + NF - 1 - lo
                    yield pair_row(m, lo), hi - lo, c, NK * (lo - c * NR) + k, NK - 1
        for c, r in enumerate(DENSE):
            if len(r):
                yield NF * (NF - 1) // 2 + r.start, len(r), c, NP, 1

    W1_PIECES = list(w1_pieces())

    ctx = ExitStack()
    with ctx:
        def sb(name, shape, dt=fp32):
            return ctx.enter_context(nc.sbuf_tensor(name, shape, dt))

        def ps(name, shape):
            return ctx.enter_context(nc.psum_tensor(name, shape, fp32))

        def sem(name):
            return ctx.enter_context(nc.semaphore(name))

        ids_sb = sb("ids_sb", [P, CH, NF], u32)
        rows = [sb(f"rows{i}", [P, NF, D]) for i in range(2)]
        rows_t = [sb(f"rows_t{i}", [D, NG, NS, PAD]) for i in range(2)]
        dots = sb("dots", [P, NF, NG])
        sym = sb("sym", [P, PAD, PITCH])
        pairs = sb("pairs", [P, NF, NK])
        z_t = sb("z_t", [P, CH, KC, P])
        h1 = sb("h1", [P, O1, P])
        h2 = sb("h2", [P, O2, P])
        y_sb = sb("y_sb", [P, CH])
        w1_sb = sb("w1_sb", [P, KC, H1])
        w2_sb = sb("w2_sb", [P, O1, H2])
        w3_sb = sb("w3_sb", [P, O2])
        b1_sb = sb("b1_sb", [P, O1])
        b2_sb = sb("b2_sb", [P, O2])
        dense_sb = sb("dense_sb", [P, CH, ND])
        dense_t = sb("dense_t", [ND, CH, P])
        ident = sb("ident", [P, P])

        ps_t = [ps(f"ps_t{i}", [P, QF, P]) for i in range(2)]
        ps_g = [ps(f"ps_g{i}", [P, STEP, P]) for i in range(2)]
        ps_act = ps("ps_act", [P, 4, P])
        ps_dve = ps("ps_dve", [P, 4, P])
        ps_z = ps_act[0:NP, 0:KC, :]
        ps_h1 = [ps_act[:, k, :] for k in range(O1 // 2)] + [ps_dve[:, k, :] for k in range(O1 // 2)]
        ps_h2 = [ps_act[:, k, :] for k in range(O2 // 2)] + [ps_dve[:, k, :] for k in range(O2 // 2)]
        ps_y = ps_dve[:, 3, 0:1]

        sym_pairs = sym[:].rearrange("p n m -> p (n m)")[:, 1:1 + NF * (PITCH + 1)].rearrange(
            "p (n k) -> p n k", k=PITCH + 1)[:, :, 0:NK]

        ids_loaded = sem("ids_loaded")
        gathered = [[sem(f"gathered{i}_{q}") for q in range(NB)] for i in range(2)]
        dense_loaded = sem("dense_loaded")
        w1_loaded = sem("w1_loaded")
        w23_loaded = sem("w23_loaded")
        biases_loaded = sem("biases_loaded")
        ident_cleared = sem("ident_cleared")
        ident_ready = sem("ident_ready")
        pads_ready = sem("pads_ready")
        dense_transposed = sem("dense_transposed")
        dense_copied = sem("dense_copied")
        dense_placed = sem("dense_placed")
        rows_transposed = sem("rows_transposed")
        rows_t_by_dve = sem("rows_t_by_dve")
        rows_t_by_act = sem("rows_t_by_act")
        products_done = sem("products_done")
        dots_by_dve = sem("dots_by_dve")
        dots_by_act = sem("dots_by_act")
        sym_blocks = sem("sym_blocks")
        pairs_ready = sem("pairs_ready")
        z_transposed = sem("z_transposed")
        z_ready = sem("z_ready")
        layer1_done = sem("layer1_done")
        h1_by_act = sem("h1_by_act")
        h1_by_dve = sem("h1_by_dve")
        layer2_done = sem("layer2_done")
        h2_by_act = sem("h2_by_act")
        h2_by_dve = sem("h2_by_dve")
        layer3_done = sem("layer3_done")
        y_copied = sem("y_copied")
        out_stored = sem("out_stored")

        block = ctx.enter_context(nc.Block())

        @block.sync
        def _(sp):
            sp.dma_start(ids_sb[:], ids.rearrange("(p c) f -> p c f", c=CH)).then_inc(ids_loaded, 16)
            sp.dma_start(dense_sb[:], dense_ctx.rearrange("(p c) f -> p c f", c=CH)).then_inc(dense_loaded, 16)
            for row, count, c, p0, step in W1_PIECES:
                sp.dma_start(w1_sb[p0:p0 + step * (count - 1) + 1:step, c, :],
                             w_top1[row:row + count, :]).then_inc(w1_loaded, 16)
            sp.dma_start(w2_sb[:], w_top2.rearrange("(p k) n -> p k n", k=O1)).then_inc(w23_loaded, 16)
            sp.dma_start(w3_sb[:], w_top3.rearrange("(p k) o -> p (k o)", k=O2)).then_inc(w23_loaded, 16)
            sp.dma_start(b1_sb[:], b_top1.rearrange("(p k) -> p k", k=O1)).then_inc(biases_loaded, 16)
            sp.dma_start(b2_sb[:], b_top2.rearrange("(p k) -> p k", k=O2)).then_inc(biases_loaded, 16)
            sp.wait_ge(dense_copied, 1)
            for k, r in enumerate(DENSE):
                if len(r):
                    sp.dma_start(z_t[NP:NP + len(r), :, k, :],
                                 dense_t[r.start:r.stop, :, :]).then_inc(dense_placed, 16)
            sp.wait_ge(y_copied, CH)
            sp.dma_start(out.rearrange("(p c) o -> p (c o)", c=CH), y_sb[:]).then_inc(out_stored, 16)
            sp.wait_ge(out_stored, 16)

        @block.gpsimd
        def _(pool):
            nc.gpsimd.memset(ident[:], 0.0).then_inc(ident_cleared, 1)
            pool.wait_ge(ident_cleared, 1)
            nc.gpsimd.affine_select(out=ident[:], in_=ident[:], compare_op=ALU.not_equal, fill=1.0, base=0,
                                    pattern=[[-1, P]], channel_multiplier=1).then_inc(ident_ready, 1)
            pool.wait_ge(ids_loaded, 16)
            for c in range(CH):
                for q, fs in enumerate(BATCHES):
                    if c >= 2:
                        pool.wait_ge(rows_transposed, NB * (c - 2) + q + 1)
                    for f in fs:
                        nc.gpsimd.indirect_dma_start(
                            out=rows[c % 2][:, f, :], out_offset=None, in_=tables[f],
                            in_offset=bass.IndirectOffsetOnAxis(ap=ids_sb[:, c, f:f + 1], axis=0),
                        ).then_inc(gathered[c % 2][q], 16)

        def copy_rows_t(copy, c, q):
            fs = BATCHES[q]
            bank = ps_t[(NB * c + q) % 2]
            return copy(rows_t[c % 2][:, :, :, fs.start:fs.stop].rearrange("d g s f -> d f s g"),
                        bank[:, 0:len(fs), :].rearrange("d f (s g) -> d f s g", s=NS))

        def copy_dots(copy, c, j, s):
            q = slice(PAD * s, PAD * (s + 1))
            return copy(dots[q, :, STEP * j:STEP * (j + 1)].rearrange("n m g -> n g m"),
                        ps_g[(NSTEP * c + j) % 2][q, :, NF * s:NF * (s + 1)])

        @block.scalar
        def _(act):
            copy = nc.scalar.copy

            def mlp(c):
                act.wait_ge(z_transposed, c + 1)
                copy(z_t[0:NP, c, :, :], ps_z).then_inc(z_ready, 1)
                if c == 0:
                    act.wait_ge(biases_loaded, 32)
                act.wait_ge(layer1_done, c + 1)
                for k in range(0, O1 // 2):
                    last = nc.scalar.activation(h1[:, k, :], ps_h1[k], ACT.Relu, bias=b1_sb[:, k:k + 1])
                last.then_inc(h1_by_act, 1)
                act.wait_ge(layer2_done, c + 1)
                for k in range(0, O2 // 2):
                    last = nc.scalar.activation(h2[:, k, :], ps_h2[k], ACT.Relu, bias=b2_sb[:, k:k + 1])
                last.then_inc(h2_by_act, 1)

            for c in range(CH):
                for q in range(NB):
                    if (NB * c + q) % 2 == 1:
                        act.wait_ge(rows_transposed, NB * c + q + 1)
                        copy_rows_t(copy, c, q).then_inc(rows_t_by_act, 1)
                    if q == 1 and c > 0:
                        mlp(c - 1)
                if c > 0:
                    act.wait_ge(sym_blocks, c)
                for j in range(NSTEP):
                    act.wait_ge(products_done, NSTEP * c + j + 1)
                    for s in range(0, NS // 2):
                        last = copy_dots(copy, c, j, s)
                    last.then_inc(dots_by_act, 1)
            mlp(CH - 1)

        @block.vector
        def _(dve):
            copy = nc.vector.tensor_copy

            def mlp(c):
                if c == 0:
                    dve.wait_ge(biases_loaded, 32)
                dve.wait_ge(layer1_done, c + 1)
                for k in range(O1 // 2, O1):
                    last = nc.vector.tensor_scalar(h1[:, k, :], ps_h1[k], b1_sb[:, k:k + 1], 0.0,
                                                   ALU.add, ALU.max)
                last.then_inc(h1_by_dve, 1)
                dve.wait_ge(layer2_done, c + 1)
                for k in range(O2 // 2, O2):
                    last = nc.vector.tensor_scalar(h2[:, k, :], ps_h2[k], b2_sb[:, k:k + 1], 0.0,
                                                   ALU.add, ALU.max)
                last.then_inc(h2_by_dve, 1)
                dve.wait_ge(layer3_done, c + 1)
                copy(y_sb[:, c:c + 1], ps_y).then_inc(y_copied, 1)

            for i in range(2):
                nc.vector.memset(rows_t[i][:, :, :, NF:PAD], 0.0).then_inc(pads_ready, 1)
            dve.wait_ge(dense_transposed, 1)
            copy(dense_t[:], ps_dve[0:ND, :, :]).then_inc(dense_copied, 1)
            for c in range(CH):
                for q in range(NB):
                    if (NB * c + q) % 2 == 0:
                        dve.wait_ge(rows_transposed, NB * c + q + 1)
                        copy_rows_t(copy, c, q).then_inc(rows_t_by_dve, 1)
                    if q == 1 and c > 0:
                        mlp(c - 1)
                if c > 0:
                    dve.wait_ge(sym_blocks, c)
                for j in range(NSTEP):
                    dve.wait_ge(products_done, NSTEP * c + j + 1)
                    for s in range(NS // 2, NS):
                        last = copy_dots(copy, c, j, s)
                    last.then_inc(dots_by_dve, 1)
                dve.wait_ge(dots_by_dve, NSTEP * (c + 1))
                dve.wait_ge(dots_by_act, NSTEP * (c + 1))
                by_m = sym[:].rearrange("p n m -> p m n")
                nc.vector.transpose(by_m[:, 0:NF, :], dots[:])
                nc.vector.transpose(by_m[:, NF:PITCH, :], dots[:, 0:NK, :]).then_inc(sym_blocks, 1)
                dve.wait_ge(sym_blocks, c + 1)
                if c > 0:
                    dve.wait_ge(z_transposed, c)
                copy(pairs[:], sym_pairs).then_inc(pairs_ready, 1)
            mlp(CH - 1)

        @block.tensor
        def _(pe):
            def transpose_rows(c, q):
                t = NB * c + q
                pe.wait_ge(gathered[c % 2][q], 16 * len(BATCHES[q]) * (c // 2 + 1))
                if t >= 2:
                    pe.wait_ge(rows_t_by_act if t % 2 else rows_t_by_dve, t // 2)
                for i, f in enumerate(BATCHES[q]):
                    last = nc.tensor.transpose(ps_t[t % 2][:, i, :], rows[c % 2][:, f, :], ident[:])
                last.then_inc(rows_transposed, 1)

            def multiply_rows(c):
                done = NB * (c + 1)
                pe.wait_ge(rows_t_by_dve, (done + 1) // 2)
                pe.wait_ge(rows_t_by_act, done // 2)
                if c < 2:
                    pe.wait_ge(pads_ready, 2)
                for j in range(NSTEP):
                    t = NSTEP * c + j
                    if t >= 2:
                        pe.wait_ge(dots_by_act, t - 1)
                        pe.wait_ge(dots_by_dve, t - 1)
                    for i in range(STEP):
                        g = STEP * j + i
                        last = nc.tensor.matmul(ps_g[t % 2][:, i, 0:NS * NF],
                                                rows_t[c % 2][:, g, :, :].rearrange("d s f -> d (s f)"),
                                                rows_t[c % 2][:, g, :, 0:NF], start=True, stop=True)
                    last.then_inc(products_done, 1)

            def mlp(c):
                pe.wait_ge(pairs_ready, c + 1)
                for k in range(KC):
                    last = nc.tensor.transpose(ps_z[:, k, :], pairs[:, NR * k:NR * (k + 1), :].rearrange("p n k -> p (n k)"), ident[:])
                last.then_inc(z_transposed, 1)
                if c == 0:
                    pe.wait_ge(dense_placed, 32)
                    pe.wait_ge(w1_loaded, 16 * len(W1_PIECES))
                pe.wait_ge(z_ready, c + 1)
                if c > 0:
                    pe.wait_ge(y_copied, c)
                for o in range(O1):
                    for k in range(KC):
                        K = KROWS[k]
                        last = nc.tensor.matmul(ps_h1[o], w1_sb[0:K, k, o:H1:O1], z_t[0:K, c, k, :],
                                                start=(k == 0), stop=(k == KC - 1))
                last.then_inc(layer1_done, 1)
                if c == 0:
                    pe.wait_ge(w23_loaded, 32)
                pe.wait_ge(h1_by_act, c + 1)
                pe.wait_ge(h1_by_dve, c + 1)
                for o in range(O2):
                    for k in range(O1):
                        last = nc.tensor.matmul(ps_h2[o], w2_sb[:, k, o:H2:O2], h1[:, k, :],
                                                start=(k == 0), stop=(k == O1 - 1))
                last.then_inc(layer2_done, 1)
                pe.wait_ge(h2_by_act, c + 1)
                pe.wait_ge(h2_by_dve, c + 1)
                for k in range(O2):
                    last = nc.tensor.matmul(ps_y, h2[:, k, :], w3_sb[:, k:k + 1],
                                            start=(k == 0), stop=(k == O2 - 1))
                last.then_inc(layer3_done, 1)

            pe.wait_ge(ident_ready, 1)
            pe.wait_ge(dense_loaded, 16)
            for c in range(CH):
                last = nc.tensor.transpose(ps_dve[0:ND, c, :], dense_sb[:, c, :], ident[:])
            last.then_inc(dense_transposed, 1)
            for c in range(CH):
                for q in range(NB):
                    transpose_rows(c, q)
                    if q == 1 and c > 0:
                        if c == 1:
                            pe.wait_ge(dense_copied, 1)
                        mlp(c - 1)
                multiply_rows(c)
            mlp(CH - 1)


def kernel(**inputs):
    import numpy as np
    import concourse.bacc as bacc
    from concourse.bass_utils import run_bass_kernel_spmd

    nc = bacc.Bacc("TRN2", target_bir_lowering=False, num_devices=1)
    arrays, aps = {}, {}
    for name, value in inputs.items():
        a = np.ascontiguousarray(value)
        arrays[f"in_{name}"] = a.view(np.uint32) if name == "ids" else a
        aps[name] = nc.dram_tensor(f"in_{name}", a.shape, mybir.dt.from_np(arrays[f"in_{name}"].dtype),
                                   kind="ExternalInput").ap()
    out = nc.dram_tensor("out", (inputs["dense_ctx"].shape[0], 1), mybir.dt.float32, kind="ExternalOutput").ap()
    dlrm_tower(nc, aps["dense_ctx"], aps["ids"], [aps[f"tbl_{f}"] for f in range(NF)],
               aps["W_top1"], aps["b_top1"], aps["W_top2"], aps["b_top2"], aps["W_top3"], out)
    return run_bass_kernel_spmd(nc, [arrays], core_ids=[0]).results[0]["out"]
```

```python
from contextlib import ExitStack

import concourse.bass as bass
from concourse import mybir

NF = 27
P = 128
ONE_HOT = (11, 12, 14, 15, 18, 19, 24, 25, 10)
FIRST_CHUNK = {10: 2}


def dlrm_tower(nc, dense_ctx, ids, tables, w_top1, b_top1, w_top2, b_top2, w_top3, out):
    fp32 = mybir.dt.float32
    fp32r = mybir.dt.float32r
    fp16 = mybir.dt.float16
    u32 = mybir.dt.uint32
    ACT = mybir.ActivationFunctionType
    ALU = mybir.AluOpType

    B, ND = dense_ctx.shape
    D = tables[0].shape[1]
    H1, H2 = w_top1.shape[1], w_top2.shape[1]
    CH = B // P
    PAD = 32
    NS = P // PAD
    NG = P // NS
    LIVE = P - PAD + NF
    STEP = 8
    NSTEP = NG // STEP
    QF = 4
    NT = len(ONE_HOT)
    FROM = [FIRST_CHUNK.get(f, 0) for f in ONE_HOT]
    GATHERED = [[f for f in range(NF) if f not in ONE_HOT or c < FIRST_CHUNK.get(f, 0)] for c in range(CH)]
    BATCHES = [[fs[i:i + QF] for i in range(0, len(fs), QF)] for fs in GATHERED]
    NB = len(BATCHES[0])
    V = tables[ONE_HOT[0]].shape[0]
    KT = 8
    VP = V // KT
    VP16 = VP // 16 * 16
    WARM = (4, 2, 2)
    RING = 8
    EARLY = 2 * NB
    NK = (NF - 1) // 2
    PITCH = NF + NK
    KC = 3
    NR = NF // KC
    NP = NR * NK
    SPARE = P - NP
    DENSE = [range(0, SPARE), range(SPARE, ND), range(ND, ND)]
    KROWS = [NP + len(r) for r in DENSE]
    O1, O2 = H1 // P, H2 // P

    def runs(features):
        found = []
        for i, f in enumerate(features):
            if found and f == found[-1][1] + found[-1][2]:
                found[-1][2] += 1
            else:
                found.append([i, f, 1])
        return found

    def pair_row(n, m):
        return n * NF - n * (n + 1) // 2 + (m - n - 1)

    def w1_pieces():
        for n in range(NF - 1):
            count = min(NK, NF - 1 - n)
            yield pair_row(n, n + 1), count, n // NR, NK * (n % NR), 1
        for m in range(NK):
            for c in range(KC):
                lo, hi = max(m + NF - NK, c * NR), min(NF, (c + 1) * NR)
                if lo < hi:
                    k = m + NF - 1 - lo
                    yield pair_row(m, lo), hi - lo, c, NK * (lo - c * NR) + k, NK - 1
        for c, r in enumerate(DENSE):
            if len(r):
                yield NF * (NF - 1) // 2 + r.start, len(r), c, NP, 1

    W1_PIECES = list(w1_pieces())

    ctx = ExitStack()
    with ctx:
        def sb(name, shape, dt=fp32):
            return ctx.enter_context(nc.sbuf_tensor(name, shape, dt))

        def ps(name, shape):
            return ctx.enter_context(nc.psum_tensor(name, shape, fp32))

        def sem(name):
            return ctx.enter_context(nc.semaphore(name))

        ids_sb = sb("ids_sb", [P, CH, NF], u32)
        rows = [sb(f"rows{i}", [P, len(GATHERED[0]), D]) for i in range(2)]
        rows_t = sb("rows_t", [D, CH, NG, NS, PAD])
        table = [sb(f"table{i}", [VP, KT, D]) for i in range(3)]
        table_hi = [sb(f"table_hi{i}", [VP, KT, D], fp32r) for i in range(3)]
        table_lo = [sb(f"table_lo{i}", [VP, KT, D], fp32r) for i in range(2)]
        one_hot = sb("one_hot", [VP, RING, B], fp32r)
        id_less_row = sb("id_less_row", [VP, NT, B], fp16)
        ids_f = sb("ids_f", [P, CH, NT])
        ids_t = sb("ids_t", [NT, B], fp16)
        pick = sb("pick", [NT, NT], fp16)
        first_row = sb("first_row", [P, 1])
        dots = sb("dots", [P, NF, NG])
        sym = sb("sym", [P, PAD, PITCH])
        pairs = sb("pairs", [P, NF, NK])
        z_t = sb("z_t", [P, CH, KC, P])
        h1 = sb("h1", [P, 2, O1, P])
        h2 = sb("h2", [P, 2, O2, P])
        y_sb = sb("y_sb", [P, CH])
        w1_sb = sb("w1_sb", [P, KC, H1])
        w2_sb = sb("w2_sb", [P, O1, H2])
        w3_sb = sb("w3_sb", [P, O2])
        b1_sb = sb("b1_sb", [P, O1])
        b2_sb = sb("b2_sb", [P, O2])
        dense_sb = sb("dense_sb", [P, CH, ND])
        dense_t = sb("dense_t", [ND, CH, P])
        ident = sb("ident", [P, P])
        nothing = sb("nothing", [P, 512], mybir.dt.bfloat16)

        ps_t = [ps(f"ps_t{i}", [P, QF, P]) for i in range(2)]
        ps_g = [ps(f"ps_g{i}", [P, STEP, P]) for i in range(2)]
        ps_rows = [ps_g[0][:, 0:4, :], ps_g[0][:, 4:8, :]]
        ps_ids = [ps_g[1][:, 0:4, :], ps_g[1][:, 4:8, :]]
        ps_act = ps("ps_act", [P, 4, P])
        ps_dve = ps("ps_dve", [P, 4, P])


        def mlp_banks(c):
            return (ps_act, ps_dve) if c < CH - 1 else (ps_g[0][:, 0:4, :], ps_g[0][:, 4:8, :])

        def ps_z(c):
            first, second = mlp_banks(c)
            return first[0:NP, 0:1, :], second[0:NP, 0:KC - 1, :]

        def ps_h(c, k, outputs):
            return mlp_banks(c)[k // (outputs // 2)][:, k % (outputs // 2), :]

        def ps_y(c):
            return mlp_banks(c)[0][:, 3, 0:1]

        Z_CHUNKS = [range(0, 1), range(1, KC)]
        Z_AT = NB - 2

        pads = rows_t[:, :, :, :, NF:PAD].rearrange("d c g s f -> d c (g s) f")
        sym_pairs = sym[:].rearrange("p n m -> p (n m)")[:, 1:1 + NF * (PITCH + 1)].rearrange(
            "p (n k) -> p n k", k=PITCH + 1)[:, :, 0:NK]

        ids_loaded = sem("ids_loaded")
        gathered = [[sem(f"gathered{i}_{q}") for q in range(NB)] for i in range(2)]
        dense_loaded = sem("dense_loaded")
        w1_loaded = sem("w1_loaded")
        w23_loaded = sem("w23_loaded")
        biases_loaded = sem("biases_loaded")
        ident_cleared = sem("ident_cleared")
        ident_ready = sem("ident_ready")
        nothing_ready = sem("nothing_ready")
        pads_ready = sem("pads_ready")
        dots_cleared = sem("dots_cleared")
        dense_transposed = sem("dense_transposed")
        dense_copied = sem("dense_copied")
        dense_placed = sem("dense_placed")
        rows_transposed = sem("rows_transposed")
        ids_converted = sem("ids_converted")
        ids_transposed = sem("ids_transposed")
        ids_t_ready = sem("ids_t_ready")
        pick_ready = sem("pick_ready")
        first_row_ready = sem("first_row_ready")
        ids_spread = sem("ids_spread")
        id_less_row_ready = sem("id_less_row_ready")
        table_loaded = [sem(f"table_loaded{i}") for i in range(3)]
        hi_ready = sem("hi_ready")
        lo_ready = sem("lo_ready")
        one_hot_ready = sem("one_hot_ready")
        one_hot_used = sem("one_hot_used")
        looked_up_copied = sem("looked_up_copied")
        products_done = sem("products_done")
        dots_by_dve = sem("dots_by_dve")
        dots_by_act = sem("dots_by_act")
        sym_blocks = sem("sym_blocks")
        pairs_ready = sem("pairs_ready")
        columns_repeated = sem("columns_repeated")
        z_transposed = sem("z_transposed")
        z_first = sem("z_first")
        z_rest = sem("z_rest")
        rows_t_copied = sem("rows_t_copied")
        layer1_done = sem("layer1_done")
        h1_first = sem("h1_first")
        h1_second = sem("h1_second")
        layer2_done = sem("layer2_done")
        h2_by_act = sem("h2_by_act")
        h2_by_dve = sem("h2_by_dve")
        layer3_done = sem("layer3_done")
        y_copied = sem("y_copied")
        out_stored = sem("out_stored")

        block = ctx.enter_context(nc.Block())

        @block.sync
        def _(sp):
            sp.dma_start(ids_sb[:], ids.rearrange("(p c) f -> p c f", c=CH)).then_inc(ids_loaded, 16)
            pieces = list(W1_PIECES)

            def load_w1(count):
                for row, count, c, p0, step in [pieces.pop(0) for _ in range(min(count, len(pieces)))]:
                    sp.dma_start(w1_sb[p0:p0 + step * (count - 1) + 1:step, c, :],
                                 w_top1[row:row + count, :]).then_inc(w1_loaded, 16)

            for t, f in enumerate(ONE_HOT):
                if t >= 3:
                    sp.wait_ge(lo_ready, t - 2)
                rows_of = tables[f].rearrange("(p k) d -> p k d", k=KT)
                sp.dma_start(table[t % 3][0:VP16], rows_of[0:VP16]).then_inc(table_loaded[t % 3], 16)
                sp.dma_start(table[t % 3][VP16:VP], rows_of[VP16:VP]).then_inc(table_loaded[t % 3], 16)
                if t == 1:
                    sp.dma_start(dense_sb[:], dense_ctx.rearrange("(p c) f -> p c f", c=CH)).then_inc(dense_loaded, 16)
                if t >= 2:
                    load_w1(6)
            load_w1(len(pieces))
            sp.dma_start(w2_sb[:], w_top2.rearrange("(p k) n -> p k n", k=O1)).then_inc(w23_loaded, 16)
            sp.dma_start(w3_sb[:], w_top3.rearrange("(p k) o -> p (k o)", k=O2)).then_inc(w23_loaded, 16)
            sp.dma_start(b1_sb[:], b_top1.rearrange("(p k) -> p k", k=O1)).then_inc(biases_loaded, 16)
            sp.dma_start(b2_sb[:], b_top2.rearrange("(p k) -> p k", k=O2)).then_inc(biases_loaded, 16)
            sp.wait_ge(dense_copied, 1)
            for k, r in enumerate(DENSE):
                if len(r):
                    sp.dma_start(z_t[NP:NP + len(r), :, k, :],
                                 dense_t[r.start:r.stop, :, :]).then_inc(dense_placed, 16)
            sp.wait_ge(y_copied, CH)
            sp.dma_start(out.rearrange("(p c) o -> p (c o)", c=CH), y_sb[:]).then_inc(out_stored, 16)
            sp.wait_ge(out_stored, 16)

        @block.gpsimd
        def _(pool):
            nc.gpsimd.memset(ident[:], 0.0).then_inc(ident_cleared, 1)
            pool.wait_ge(ident_cleared, 1)
            nc.gpsimd.affine_select(out=ident[:], in_=ident[:], compare_op=ALU.not_equal, fill=1.0, base=0,
                                    pattern=[[-1, P]], channel_multiplier=1).then_inc(ident_ready, 1)
            nc.gpsimd.iota(first_row[:], pattern=[[0, 1]], base=0, channel_multiplier=-KT,
                           allow_small_or_imprecise_dtypes=True).then_inc(first_row_ready, 1)
            nc.gpsimd.memset(pads[:, CH // 2:CH], 0.0).then_inc(pads_ready, 1)
            pool.wait_ge(ids_loaded, 16)
            for c in range(CH):
                for q, fs in enumerate(BATCHES[c]):
                    if c >= 2:
                        pool.wait_ge(rows_transposed, NB * (c - 2) + q + 1)
                    for i, f in enumerate(fs):
                        nc.gpsimd.indirect_dma_start(
                            out=rows[c % 2][:, QF * q + i, :], out_offset=None, in_=tables[f],
                            in_offset=bass.IndirectOffsetOnAxis(ap=ids_sb[:, c, f:f + 1], axis=0),
                        ).then_inc(gathered[c % 2][q], 16)

        def copy_dots(copy, c, j, s):
            q = slice(PAD * s, PAD * s + NF)
            return copy(dots[q, :, STEP * j:STEP * (j + 1)].rearrange("n m g -> n g m"),
                        ps_g[(NSTEP * c + j) % 2][q, :, NF * s:NF * (s + 1)])

        def repeat_columns(copy):
            return copy(sym[:, NF - NK:NF, NF:PITCH], sym[:, NF - NK:NF, 0:NK])

        @block.scalar
        def _(act):
            copy = nc.scalar.copy

            def copy_z(c):
                act.wait_ge(z_transposed, 2 * c + 1)
                copy(z_t[0:NP, c, 0:1, :], ps_z(c)[0]).then_inc(z_first, 1)

            def relu1(c):
                if c == 0:
                    act.wait_ge(biases_loaded, 32)
                act.wait_ge(layer1_done, 2 * c + 1)
                for k in range(0, O1 // 2):
                    last = nc.scalar.activation(h1[:, c % 2, k, :], ps_h(c, k, O1), ACT.Relu, bias=b1_sb[:, k:k + 1])
                last.then_inc(h1_first, 1)

            def relu1_second(c):
                act.wait_ge(layer1_done, 2 * c + 2)
                for k in range(O1 // 2, O1):
                    last = nc.scalar.activation(h1[:, c % 2, k, :], ps_h(c, k, O1), ACT.Relu, bias=b1_sb[:, k:k + 1])
                last.then_inc(h1_second, 1)

            def relu2(c):
                act.wait_ge(layer2_done, 2 * c + 1)
                for k in range(0, O2 // 2):
                    last = nc.scalar.activation(h2[:, c % 2, k, :], ps_h(c, k, O2), ACT.Relu, bias=b2_sb[:, k:k + 1])
                last.then_inc(h2_by_act, 1)

            def copy_y(c):
                act.wait_ge(layer3_done, c + 1)
                copy(y_sb[:, c:c + 1], ps_y(c)).then_inc(y_copied, 1)

            def split_hi(t):
                act.wait_ge(table_loaded[t % 3], 32 * (t // 3 + 1))
                if t >= 3:
                    act.wait_ge(one_hot_used, KT * (t - 2))
                copy(table_hi[t % 3][:], table[t % 3][:]).then_inc(hi_ready, 1)

            def subtract_first_row(t):
                act.wait_ge(ids_spread, t + 1)
                nc.scalar.activation(id_less_row[:, t, P * FROM[t]:],
                                     ps_ids[t % 2][0:VP, FROM[t]:, :].rearrange("p c b -> p (c b)"),
                                     ACT.Identity, bias=first_row[0:VP, 0:1]).then_inc(id_less_row_ready, 1)

            def copy_looked_up(t):
                act.wait_ge(one_hot_used, KT * (t + 1))
                copy(rows_t[:, FROM[t]:, :, :, ONE_HOT[t]].rearrange("d c g s -> d c s g"),
                     ps_rows[t % 2][:, FROM[t]:, :].rearrange("d c (s g) -> d c s g", s=NS)).then_inc(looked_up_copied, 1)

            def copy_rows_t(b):
                c, q = divmod(b, NB)
                act.wait_ge(rows_transposed, b + 1)
                for i, f, n in runs(BATCHES[c][q]):
                    last = copy(rows_t[:, c, :, :, f:f + n].rearrange("d g s f -> d f s g"),
                                ps_t[b % 2][:, i:i + n, :].rearrange("d f (s g) -> d f s g", s=NS))
                last.then_inc(rows_t_copied, 1)

            act.wait_ge(ids_transposed, 1)
            copy(ids_t[:], ps_t[0][0:NT, :, :].rearrange("t c p -> t (c p)")).then_inc(ids_t_ready, 1)
            act.wait_ge(first_row_ready, 1)
            split_hi(0)
            subtract_first_row(0)
            subtract_first_row(1)
            split_hi(1)
            for t in range(NT):
                if t + 2 < NT:
                    subtract_first_row(t + 2)
                    split_hi(t + 2)
                copy_looked_up(t)
                if t >= 1:
                    copy_rows_t(t - 1)
            def dots_step(c, j):
                if c > 0 and j == 0:
                    act.wait_ge(sym_blocks, c)
                if (c, j) == (0, 0):
                    act.wait_ge(dots_cleared, 1)
                act.wait_ge(products_done, NSTEP * c + j + 1)
                for s in range(0, NS // 2):
                    last = copy_dots(copy, c, j, s)
                last.then_inc(dots_by_act, 1)

            for b in range(NT - 1, 2 * NB - 1):
                copy_rows_t(b)
            dots_step(0, 0)
            dots_step(0, 1)
            copy_rows_t(2 * NB - 1)
            dots_step(0, 2)
            dots_step(0, 3)
            dots_step(1, 0)
            dots_step(1, 1)
            copy_z(0)
            dots_step(1, 2)
            relu1(0)
            copy_rows_t(2 * NB)
            dots_step(1, 3)
            copy_rows_t(2 * NB + 1)
            copy_rows_t(2 * NB + 2)
            relu2(0)
            copy_rows_t(2 * NB + 3)
            copy_y(0)
            copy_rows_t(2 * NB + 4)
            copy_z(1)
            dots_step(2, 0)
            copy_rows_t(3 * NB)
            dots_step(2, 1)
            relu1(1)
            dots_step(2, 2)
            copy_rows_t(3 * NB + 1)
            dots_step(2, 3)
            copy_rows_t(3 * NB + 2)
            relu2(1)
            copy_y(1)
            copy_z(2)
            copy_rows_t(3 * NB + 3)
            relu1(2)
            copy_rows_t(3 * NB + 4)
            for j in range(NSTEP):
                dots_step(3, j)
            relu1_second(2)
            act.wait_ge(sym_blocks, CH)
            repeat_columns(copy).then_inc(columns_repeated, 1)
            copy_z(3)
            relu1(3)
            relu2(2)
            relu2(3)
            copy_y(2)
            copy_y(3)

        @block.vector
        def _(dve):
            copy = nc.vector.tensor_copy

            def copy_z(c):
                dve.wait_ge(z_transposed, 2 * c + 2)
                copy(z_t[0:NP, c, 1:KC, :], ps_z(c)[1]).then_inc(z_rest, 1)

            def relu1(c):
                if c == 0:
                    dve.wait_ge(biases_loaded, 32)
                dve.wait_ge(layer1_done, 2 * c + 2)
                for k in range(O1 // 2, O1):
                    last = nc.vector.tensor_scalar(h1[:, c % 2, k, :], ps_h(c, k, O1), b1_sb[:, k:k + 1], 0.0,
                                                   ALU.add, ALU.max)
                last.then_inc(h1_second, 1)

            def relu2(c):
                dve.wait_ge(layer2_done, 2 * c + 2)
                for k in range(O2 // 2, O2):
                    last = nc.vector.tensor_scalar(h2[:, c % 2, k, :], ps_h(c, k, O2), b2_sb[:, k:k + 1], 0.0,
                                                   ALU.add, ALU.max)
                last.then_inc(h2_by_dve, 1)

            nc.vector.memset(nothing[:], 0.0).then_inc(nothing_ready, 1)
            nc.vector.memset(dots[:], 0.0).then_inc(dots_cleared, 1)
            nc.vector.memset(pads[:, 0:CH // 2], 0.0).then_inc(pads_ready, 1)
            dve.wait_ge(ident_ready, 1)
            copy(pick[:], ident[0:NT, 0:NT]).then_inc(pick_ready, 1)
            dve.wait_ge(ids_loaded, 16)
            for i, f, n in runs(ONE_HOT):
                last = copy(ids_f[:, :, i:i + n], ids_sb[:, :, f:f + n])
            last.then_inc(ids_converted, 1)
            for t in range(NT):
                dve.wait_ge(hi_ready, t + 1)
                dve.wait_ge(table_loaded[t % 3], 32 * (t // 3 + 1))
                if t >= 2:
                    dve.wait_ge(one_hot_used, KT * (t - 1))
                nc.vector.tensor_tensor(table_lo[t % 2][:], table[t % 3][:], table_hi[t % 3][:].bitcast(fp32),
                                        ALU.subtract).then_inc(lo_ready, 1)
                dve.wait_ge(id_less_row_ready, t + 1)
                for k in range(KT):
                    i = KT * t + k
                    if i >= RING:
                        dve.wait_ge(one_hot_used, i - RING + 1)
                    nc.vector.tensor_scalar(one_hot[:, i % RING, P * FROM[t]:], id_less_row[:, t, P * FROM[t]:], float(k), None,
                                            ALU.is_equal).then_inc(one_hot_ready, 1)
                if t == 1:
                    dve.wait_ge(dense_transposed, 1)
                    copy(dense_t[:], ps_dve[0:ND, :, :]).then_inc(dense_copied, 1)

            def dots_step(c, j):
                if (c, j) == (0, 0):
                    dve.wait_ge(dots_cleared, 1)
                dve.wait_ge(products_done, NSTEP * c + j + 1)
                for s in range(NS // 2, NS):
                    last = copy_dots(copy, c, j, s)
                last.then_inc(dots_by_dve, 1)

            def pick_pairs(c):
                dve.wait_ge(dots_by_dve, NSTEP * (c + 1))
                dve.wait_ge(dots_by_act, NSTEP * (c + 1))
                nc.vector.transpose(sym[:].rearrange("p n m -> p m n")[:, 0:NF, :], dots[:]).then_inc(sym_blocks, 1)
                dve.wait_ge(sym_blocks, c + 1)
                if c > 0:
                    dve.wait_ge(z_transposed, 2 * c)
                if c < CH - 1:
                    repeat_columns(copy).then_inc(columns_repeated, 1)
                copy(pairs[:, 0:NF - NK, :], sym_pairs[:, 0:NF - NK, :])
                dve.wait_ge(columns_repeated, c + 1)
                copy(pairs[:, NF - NK:NF, :], sym_pairs[:, NF - NK:NF, :]).then_inc(pairs_ready, 1)

            for j in range(NSTEP):
                dots_step(0, j)
            pick_pairs(0)
            dots_step(1, 0)
            dots_step(1, 1)
            copy_z(0)
            dots_step(1, 2)
            relu1(0)
            dots_step(1, 3)
            pick_pairs(1)
            relu2(0)
            copy_z(1)
            dots_step(2, 0)
            dots_step(2, 1)
            dots_step(2, 2)
            relu1(1)
            dots_step(2, 3)
            pick_pairs(2)
            relu2(1)
            copy_z(2)
            for j in range(NSTEP):
                dots_step(3, j)
            pick_pairs(3)
            copy_z(3)
            relu1(3)
            relu2(2)
            relu2(3)

        @block.tensor
        def _(pe):
            def spread_ids(t):
                if t >= 2:
                    pe.wait_ge(id_less_row_ready, t - 1)
                nc.tensor.matmul(ps_ids[t % 2][:, FROM[t]:, :].rearrange("p c b -> p (c b)"),
                                 pick[:, t:t + 1].to_broadcast([NT, P]), ids_t[:, P * FROM[t]:],
                                 start=True, stop=True).then_inc(ids_spread, 1)

            def look_up(t):
                pe.wait_ge(hi_ready, t + 1)
                pe.wait_ge(lo_ready, t + 1)
                if t >= 2:
                    pe.wait_ge(looked_up_copied, t - 1)
                bank = ps_rows[t % 2][:, FROM[t]:, :].rearrange("d c b -> d (c b)")
                for k in range(KT):
                    i = KT * t + k
                    pe.wait_ge(one_hot_ready, i + 1)
                    nc.tensor.matmul(bank, table_hi[t % 3][:, k, :], one_hot[:, i % RING, P * FROM[t]:],
                                     start=(k == 0), stop=False)
                    last = nc.tensor.matmul(bank, table_lo[t % 2][:, k, :], one_hot[:, i % RING, P * FROM[t]:],
                                            start=False, stop=(k == KT - 1))
                    last.then_inc(one_hot_used, 1)

            def transpose_rows(b):
                c, q = divmod(b, NB)
                pe.wait_ge(gathered[c % 2][q], 16 * sum(len(BATCHES[e][q]) for e in range(c % 2, c + 1, 2)))
                if b >= 2:
                    pe.wait_ge(rows_t_copied, b - 1)
                for i in range(len(BATCHES[c][q])):
                    last = nc.tensor.transpose(ps_t[b % 2][:, i, :], rows[c % 2][:, QF * q + i, :], ident[:])
                last.then_inc(rows_transposed, 1)

            def multiply_rows(c, j):
                if j == 0:
                    pe.wait_ge(rows_t_copied, NB * (c + 1))
                    if c == 0:
                        pe.wait_ge(looked_up_copied, NT)
                        pe.wait_ge(pads_ready, 2)
                t = NSTEP * c + j
                if t >= 2:
                    pe.wait_ge(dots_by_act, t - 1)
                    pe.wait_ge(dots_by_dve, t - 1)
                for i in range(STEP):
                    g = STEP * j + i
                    last = nc.tensor.matmul(ps_g[t % 2][0:LIVE, i, 0:NS * NF],
                                            rows_t[:, c, g, :, :].rearrange("d s f -> d (s f)")[:, 0:LIVE],
                                            rows_t[:, c, g, :, 0:NF], start=True, stop=True)
                last.then_inc(products_done, 1)

            def transpose_pairs(c):
                pe.wait_ge(pairs_ready, c + 1)
                if 0 < c < CH - 1:
                    pe.wait_ge(y_copied, c)
                for bank, ks in zip(ps_z(c), Z_CHUNKS):
                    for j, k in enumerate(ks):
                        last = nc.tensor.transpose(bank[:, j, :],
                                                   pairs[:, NR * k:NR * (k + 1), :].rearrange("p n k -> p (n k)"),
                                                   ident[:])
                    last.then_inc(z_transposed, 1)

            def layer1(c, half):
                if half == 0:
                    if c == 0:
                        pe.wait_ge(dense_copied, 1)
                        pe.wait_ge(dense_placed, 32)
                        pe.wait_ge(w1_loaded, 16 * len(W1_PIECES))
                for o in range(O1 // 2 * half, O1 // 2 * (half + 1)):
                    for k in range(KC):
                        if o == 0 and k == 0:
                            pe.wait_ge(z_first, c + 1)
                        if o == 0 and k == 1:
                            pe.wait_ge(z_rest, c + 1)
                        K = KROWS[k]
                        last = nc.tensor.matmul(ps_h(c, o, O1), w1_sb[0:K, k, o:H1:O1], z_t[0:K, c, k, :],
                                                start=(k == 0), stop=(k == KC - 1))
                last.then_inc(layer1_done, 1)

            def layer2(c, o):
                if c == 0:
                    pe.wait_ge(w23_loaded, 32)
                pe.wait_ge(h1_first, c + 1)
                for k in range(O1):
                    if k == O1 // 2:
                        pe.wait_ge(h1_second, c + 1)
                    last = nc.tensor.matmul(ps_h(c, o, O2), w2_sb[:, k, o:H2:O2], h1[:, c % 2, k, :],
                                            start=(k == 0), stop=(k == O1 - 1))
                last.then_inc(layer2_done, 1)

            def layer3(c):
                for k in range(O2):
                    pe.wait_ge(h2_by_dve if k else h2_by_act, c + 1)
                    last = nc.tensor.matmul(ps_y(c), h2[:, c % 2, k, :], w3_sb[:, k:k + 1],
                                            start=(k == 0), stop=(k == O2 - 1))
                last.then_inc(layer3_done, 1)

            pe.wait_ge(ident_ready, 1)
            def keep_busy(count):
                for _ in range(count):
                    nc.tensor.matmul(ps_g[0][:, 0:4, :].rearrange("p c b -> p (c b)"), nothing[:, 0:P], nothing[:],
                                     start=True, stop=True)

            pe.wait_ge(nothing_ready, 1)
            keep_busy(WARM[0])
            pe.wait_ge(ids_converted, 1)
            for c in range(CH):
                last = nc.tensor.transpose(ps_t[0][0:NT, c, :], ids_f[:, c, :], ident[:])
            last.then_inc(ids_transposed, 1)
            keep_busy(WARM[1])
            pe.wait_ge(ids_t_ready, 1)
            pe.wait_ge(pick_ready, 1)
            spread_ids(0)
            spread_ids(1)
            pe.wait_ge(dense_loaded, 16)
            for c in range(CH):
                last = nc.tensor.transpose(ps_dve[0:ND, c, :], dense_sb[:, c, :], ident[:])
            last.then_inc(dense_transposed, 1)
            keep_busy(WARM[2])
            for t in range(NT):
                look_up(t)
                if t + 2 < NT:
                    spread_ids(t + 2)
                if t >= 1:
                    transpose_rows(t - 1)
            for b in range(NT - 1, 2 * NB - 1):
                transpose_rows(b)
            multiply_rows(0, 0)
            multiply_rows(0, 1)
            transpose_rows(2 * NB - 1)
            multiply_rows(0, 2)
            multiply_rows(0, 3)
            multiply_rows(1, 0)
            multiply_rows(1, 1)
            transpose_pairs(0)
            multiply_rows(1, 2)
            layer1(0, 0)
            transpose_rows(2 * NB)
            layer1(0, 1)
            multiply_rows(1, 3)
            transpose_rows(2 * NB + 1)
            transpose_rows(2 * NB + 2)
            layer2(0, 0)
            layer2(0, 1)
            transpose_rows(2 * NB + 3)
            layer3(0)
            transpose_rows(2 * NB + 4)
            transpose_pairs(1)
            multiply_rows(2, 0)
            transpose_rows(3 * NB)
            multiply_rows(2, 1)
            layer1(1, 0)
            multiply_rows(2, 2)
            layer1(1, 1)
            transpose_rows(3 * NB + 1)
            multiply_rows(2, 3)
            transpose_rows(3 * NB + 2)
            layer2(1, 0)
            layer2(1, 1)
            layer3(1)
            transpose_pairs(2)
            transpose_rows(3 * NB + 3)
            layer1(2, 0)
            transpose_rows(3 * NB + 4)
            for j in range(NSTEP):
                multiply_rows(3, j)
            layer1(2, 1)
            layer2(2, 0)
            transpose_pairs(3)
            layer1(3, 0)
            layer1(3, 1)
            layer2(2, 1)
            layer2(3, 0)
            layer2(3, 1)
            layer3(2)
            layer3(3)


def kernel(**inputs):
    import numpy as np
    import concourse.bacc as bacc
    from concourse.bass_utils import run_bass_kernel_spmd

    nc = bacc.Bacc("TRN2", target_bir_lowering=False, num_devices=1)
    arrays, aps = {}, {}
    for name, value in inputs.items():
        a = np.ascontiguousarray(value)
        arrays[f"in_{name}"] = a.view(np.uint32) if name == "ids" else a
        aps[name] = nc.dram_tensor(f"in_{name}", a.shape, mybir.dt.from_np(arrays[f"in_{name}"].dtype),
                                   kind="ExternalInput").ap()
    out = nc.dram_tensor("out", (inputs["dense_ctx"].shape[0], 1), mybir.dt.float32, kind="ExternalOutput").ap()
    dlrm_tower(nc, aps["dense_ctx"], aps["ids"], [aps[f"tbl_{f}"] for f in range(NF)],
               aps["W_top1"], aps["b_top1"], aps["W_top2"], aps["b_top2"], aps["W_top3"], out)
    return run_bass_kernel_spmd(nc, [arrays], core_ids=[0]).results[0]["out"]
```

```python
from contextlib import ExitStack

import concourse.bass as bass
from concourse import mybir

NF = 27
P = 128
ONE_HOT = (10, 11, 12, 14, 15, 18, 19, 24, 25)


def dlrm_tower(nc, dense_ctx, ids, tables, w_top1, b_top1, w_top2, b_top2, w_top3, out):
    fp32 = mybir.dt.float32
    fp32r = mybir.dt.float32r
    fp16 = mybir.dt.float16
    u32 = mybir.dt.uint32
    ACT = mybir.ActivationFunctionType
    ALU = mybir.AluOpType

    B, ND = dense_ctx.shape
    D = tables[0].shape[1]
    H1, H2 = w_top1.shape[1], w_top2.shape[1]
    CH = B // P
    PAD = 32
    NS = P // PAD
    NG = P // NS
    LIVE = P - PAD + NF
    STEP = 8
    NSTEP = NG // STEP
    QF = 4
    NT = len(ONE_HOT)
    GATHERED = [f for f in range(NF) if f not in ONE_HOT]
    BATCHES = [GATHERED[i:i + QF] for i in range(0, len(GATHERED), QF)]
    NB = len(BATCHES)
    assert CH == 4 and NB == 5
    V = tables[ONE_HOT[0]].shape[0]
    KT = 8
    VP = V // KT
    VP16 = VP // 16 * 16
    WARM = (5, 2)
    RING = 8
    NK = (NF - 1) // 2
    PITCH = NF + NK
    KC = 3
    NR = NF // KC
    NP = NR * NK
    SPARE = P - NP
    DENSE = [range(0, SPARE), range(SPARE, ND), range(ND, ND)]
    KROWS = [NP + len(r) for r in DENSE]
    O1, O2 = H1 // P, H2 // P

    def runs(features):
        found = []
        for i, f in enumerate(features):
            if found and f == found[-1][1] + found[-1][2]:
                found[-1][2] += 1
            else:
                found.append([i, f, 1])
        return found

    def pair_row(n, m):
        return n * NF - n * (n + 1) // 2 + (m - n - 1)

    def w1_pieces():
        for n in range(NF - 1):
            count = min(NK, NF - 1 - n)
            yield pair_row(n, n + 1), count, n // NR, NK * (n % NR), 1
        for m in range(NK):
            for c in range(KC):
                lo, hi = max(m + NF - NK, c * NR), min(NF, (c + 1) * NR)
                if lo < hi:
                    k = m + NF - 1 - lo
                    yield pair_row(m, lo), hi - lo, c, NK * (lo - c * NR) + k, NK - 1
        for c, r in enumerate(DENSE):
            if len(r):
                yield NF * (NF - 1) // 2 + r.start, len(r), c, NP, 1

    W1_PIECES = list(w1_pieces())

    ctx = ExitStack()
    with ctx:
        def sb(name, shape, dt=fp32):
            return ctx.enter_context(nc.sbuf_tensor(name, shape, dt))

        def ps(name, shape):
            return ctx.enter_context(nc.psum_tensor(name, shape, fp32))

        def sem(name):
            return ctx.enter_context(nc.semaphore(name))

        ids_sb = sb("ids_sb", [P, CH, NF], u32)
        rows = [sb(f"rows{i}", [P, len(GATHERED), D]) for i in range(2)]
        rows_t = sb("rows_t", [D, CH, NG, NS, PAD])
        table = [sb(f"table{i}", [VP, KT, D]) for i in range(3)]
        table_hi = [sb(f"table_hi{i}", [VP, KT, D], fp32r) for i in range(3)]
        table_lo = [sb(f"table_lo{i}", [VP, KT, D], fp32r) for i in range(2)]
        one_hot = sb("one_hot", [VP, RING, B], fp32r)
        id_less_row = sb("id_less_row", [VP, NT, B], fp16)
        ids_f = sb("ids_f", [P, CH, NT])
        ids_t = sb("ids_t", [NT, B], fp16)
        pick = sb("pick", [NT, NT], fp16)
        first_row = sb("first_row", [P, 1])
        dots = sb("dots", [P, NF, NG])
        sym = sb("sym", [P, PAD, PITCH])
        pairs = sb("pairs", [P, NF, NK])
        z_t = sb("z_t", [P, CH, KC, P])
        h1 = sb("h1", [P, 2, O1, P])
        h2 = sb("h2", [P, 2, O2, P])
        y_sb = sb("y_sb", [P, CH])
        w1_sb = sb("w1_sb", [P, KC, H1])
        w2_sb = sb("w2_sb", [P, O1, H2])
        w3_sb = sb("w3_sb", [P, O2])
        b1_sb = sb("b1_sb", [P, O1])
        b2_sb = sb("b2_sb", [P, O2])
        dense_sb = sb("dense_sb", [P, CH, ND])
        dense_t = sb("dense_t", [ND, CH, P])
        ident = sb("ident", [P, P])
        nothing = sb("nothing", [P, 512], mybir.dt.bfloat16)

        ps_t = [ps(f"ps_t{i}", [P, QF, P]) for i in range(2)]
        ps_g = [ps(f"ps_g{i}", [P, STEP, P]) for i in range(2)]
        ps_rows = [ps_g[0][:, 0:4, :], ps_g[0][:, 4:8, :]]
        ps_ids = [ps_g[1][:, 0:4, :], ps_g[1][:, 4:8, :]]
        ps_act = ps("ps_act", [P, 4, P])
        ps_dve = ps("ps_dve", [P, 4, P])

        def mlp_banks(c):
            return (ps_act, ps_dve) if c < CH - 1 else (ps_g[0][:, 0:4, :], ps_g[0][:, 4:8, :])

        def ps_z(c):
            first, second = mlp_banks(c)
            return first[0:NP, 0:1, :], second[0:NP, 0:KC - 1, :]

        def ps_h(c, k, outputs):
            return mlp_banks(c)[k // (outputs // 2)][:, k % (outputs // 2), :]

        def ps_y(c):
            return mlp_banks(c)[0][:, 3, 0:1]

        Z_CHUNKS = [range(0, 1), range(1, KC)]

        pads = rows_t[:, :, :, :, NF:PAD].rearrange("d c g s f -> d c (g s) f")
        sym_pairs = sym[:].rearrange("p n m -> p (n m)")[:, 1:1 + NF * (PITCH + 1)].rearrange(
            "p (n k) -> p n k", k=PITCH + 1)[:, :, 0:NK]

        ids_loaded = sem("ids_loaded")
        gathered = [[sem(f"gathered{i}_{q}") for q in range(NB)] for i in range(2)]
        dense_loaded = sem("dense_loaded")
        w1_loaded = sem("w1_loaded")
        w23_loaded = sem("w23_loaded")
        biases_loaded = sem("biases_loaded")
        ident_cleared = sem("ident_cleared")
        ident_ready = sem("ident_ready")
        nothing_ready = sem("nothing_ready")
        pads_ready = sem("pads_ready")
        dots_cleared = sem("dots_cleared")
        dense_transposed = sem("dense_transposed")
        dense_copied = sem("dense_copied")
        dense_placed = sem("dense_placed")
        rows_transposed = sem("rows_transposed")
        ids_converted = sem("ids_converted")
        ids_transposed = sem("ids_transposed")
        ids_t_ready = sem("ids_t_ready")
        pick_ready = sem("pick_ready")
        first_row_ready = sem("first_row_ready")
        ids_spread = sem("ids_spread")
        id_less_row_ready = sem("id_less_row_ready")
        table_loaded = [sem(f"table_loaded{i}") for i in range(3)]
        first_hi_ready = sem("first_hi_ready")
        hi_ready = sem("hi_ready")
        lo_ready = sem("lo_ready")
        one_hot_ready = sem("one_hot_ready")
        one_hot_used = sem("one_hot_used")
        looked_up_copied = sem("looked_up_copied")
        products_done = sem("products_done")
        dots_by_dve = sem("dots_by_dve")
        dots_by_act = sem("dots_by_act")
        sym_blocks = sem("sym_blocks")
        pairs_ready = sem("pairs_ready")
        columns_repeated = sem("columns_repeated")
        z_transposed = sem("z_transposed")
        z_first = sem("z_first")
        z_rest = sem("z_rest")
        rows_t_copied = sem("rows_t_copied")
        layer1_done = sem("layer1_done")
        h1_first = sem("h1_first")
        h1_second = sem("h1_second")
        layer2_done = sem("layer2_done")
        h2_first = sem("h2_first")
        h2_second = sem("h2_second")
        layer3_done = sem("layer3_done")
        y_copied = sem("y_copied")
        out_stored = sem("out_stored")

        block = ctx.enter_context(nc.Block())

        @block.sync
        def _(sp):
            sp.dma_start(ids_sb[:], ids.rearrange("(p c) f -> p c f", c=CH)).then_inc(ids_loaded, 16)
            pieces = list(W1_PIECES)

            def load_w1(count):
                for row, count, c, p0, step in [pieces.pop(0) for _ in range(min(count, len(pieces)))]:
                    sp.dma_start(w1_sb[p0:p0 + step * (count - 1) + 1:step, c, :],
                                 w_top1[row:row + count, :]).then_inc(w1_loaded, 16)

            for t, f in enumerate(ONE_HOT):
                if t >= 3:
                    sp.wait_ge(lo_ready, t - 2)
                rows_of = tables[f].rearrange("(p k) d -> p k d", k=KT)
                sp.dma_start(table[t % 3][0:VP16], rows_of[0:VP16]).then_inc(table_loaded[t % 3], 16)
                sp.dma_start(table[t % 3][VP16:VP], rows_of[VP16:VP]).then_inc(table_loaded[t % 3], 16)
                if t == 1:
                    sp.dma_start(dense_sb[:], dense_ctx.rearrange("(p c) f -> p c f", c=CH)).then_inc(
                        dense_loaded, 16)
                if t >= 2:
                    load_w1(6)
            load_w1(len(pieces))
            sp.dma_start(w2_sb[:], w_top2.rearrange("(p k) n -> p k n", k=O1)).then_inc(w23_loaded, 16)
            sp.dma_start(w3_sb[:], w_top3.rearrange("(p k) o -> p (k o)", k=O2)).then_inc(w23_loaded, 16)
            sp.dma_start(b1_sb[:], b_top1.rearrange("(p k) -> p k", k=O1)).then_inc(biases_loaded, 16)
            sp.dma_start(b2_sb[:], b_top2.rearrange("(p k) -> p k", k=O2)).then_inc(biases_loaded, 16)
            sp.wait_ge(dense_copied, 1)
            for k, r in enumerate(DENSE):
                if len(r):
                    sp.dma_start(z_t[NP:NP + len(r), :, k, :],
                                 dense_t[r.start:r.stop, :, :]).then_inc(dense_placed, 16)
            sp.wait_ge(y_copied, CH)
            sp.dma_start(out.rearrange("(p c) o -> p (c o)", c=CH), y_sb[:]).then_inc(out_stored, 16)
            sp.wait_ge(out_stored, 16)

        @block.gpsimd
        def _(pool):
            nc.gpsimd.memset(ident[:], 0.0).then_inc(ident_cleared, 1)
            pool.wait_ge(ident_cleared, 1)
            nc.gpsimd.affine_select(out=ident[:], in_=ident[:], compare_op=ALU.not_equal, fill=1.0, base=0,
                                    pattern=[[-1, P]], channel_multiplier=1).then_inc(ident_ready, 1)
            nc.gpsimd.iota(first_row[:], pattern=[[0, 1]], base=0, channel_multiplier=-KT,
                           allow_small_or_imprecise_dtypes=True).then_inc(first_row_ready, 1)
            nc.gpsimd.memset(pads[:, CH // 2:CH], 0.0).then_inc(pads_ready, 1)
            pool.wait_ge(ids_loaded, 16)
            for c in range(CH):
                for q, fs in enumerate(BATCHES):
                    if c >= 2:
                        pool.wait_ge(rows_transposed, NB * (c - 2) + q + 1)
                    for i, f in enumerate(fs):
                        nc.gpsimd.indirect_dma_start(
                            out=rows[c % 2][:, QF * q + i, :], out_offset=None, in_=tables[f],
                            in_offset=bass.IndirectOffsetOnAxis(ap=ids_sb[:, c, f:f + 1], axis=0),
                        ).then_inc(gathered[c % 2][q], 16)

        def wait_for_hi(engine, t):
            if t == 0:
                engine.wait_ge(first_hi_ready, 1)
            else:
                engine.wait_ge(hi_ready, t)

        def copy_dots(copy, c, j, s):
            q = slice(PAD * s, PAD * s + NF)
            return copy(dots[q, :, STEP * j:STEP * (j + 1)].rearrange("n m g -> n g m"),
                        ps_g[(NSTEP * c + j) % 2][q, :, NF * s:NF * (s + 1)])

        def repeat_columns(copy):
            return copy(sym[:, NF - NK:NF, NF:PITCH], sym[:, NF - NK:NF, 0:NK])

        @block.scalar
        def _(act):
            copy = nc.scalar.copy

            def copy_z(c):
                act.wait_ge(z_transposed, 2 * c + 1)
                copy(z_t[0:NP, c, 0:1, :], ps_z(c)[0]).then_inc(z_first, 1)

            def relu1(c):
                if c == 0:
                    act.wait_ge(biases_loaded, 32)
                act.wait_ge(layer1_done, O1 * c + O1 // 2)
                for k in range(0, O1 // 2):
                    last = nc.scalar.activation(h1[:, c % 2, k, :], ps_h(c, k, O1), ACT.Relu,
                                                bias=b1_sb[:, k:k + 1])
                last.then_inc(h1_first, 1)

            def relu1_second(c):
                act.wait_ge(layer1_done, O1 * (c + 1))
                for k in range(O1 // 2, O1):
                    last = nc.scalar.activation(h1[:, c % 2, k, :], ps_h(c, k, O1), ACT.Relu,
                                                bias=b1_sb[:, k:k + 1])
                last.then_inc(h1_second, 1)

            def relu2(c):
                act.wait_ge(layer2_done, 2 * c + 1)
                for k in range(0, O2 // 2):
                    last = nc.scalar.activation(h2[:, c % 2, k, :], ps_h(c, k, O2), ACT.Relu,
                                                bias=b2_sb[:, k:k + 1])
                last.then_inc(h2_first, 1)

            def relu2_second(c):
                act.wait_ge(layer2_done, 2 * c + 2)
                for k in range(O2 // 2, O2):
                    last = nc.scalar.activation(h2[:, c % 2, k, :], ps_h(c, k, O2), ACT.Relu,
                                                bias=b2_sb[:, k:k + 1])
                last.then_inc(h2_second, 1)

            def copy_y(c):
                act.wait_ge(layer3_done, c + 1)
                copy(y_sb[:, c:c + 1], ps_y(c)).then_inc(y_copied, 1)

            def split_hi(t):
                act.wait_ge(table_loaded[t % 3], 32 * (t // 3 + 1))
                if t >= 3:
                    act.wait_ge(one_hot_used, KT * (t - 2))
                copy(table_hi[t % 3][:], table[t % 3][:]).then_inc(hi_ready, 1)

            def subtract_first_row(t):
                act.wait_ge(ids_spread, t + 1)
                nc.scalar.activation(id_less_row[:, t, :],
                                     ps_ids[t % 2][0:VP].rearrange("p c b -> p (c b)"),
                                     ACT.Identity, bias=first_row[0:VP, 0:1]).then_inc(id_less_row_ready, 1)

            def copy_looked_up(t):
                act.wait_ge(one_hot_used, KT * (t + 1))
                copy(rows_t[:, :, :, :, ONE_HOT[t]].rearrange("d c g s -> d c s g"),
                     ps_rows[t % 2].rearrange("d c (s g) -> d c s g", s=NS)).then_inc(looked_up_copied, 1)

            def copy_rows_t(b):
                c, q = divmod(b, NB)
                act.wait_ge(rows_transposed, b + 1)
                for i, f, n in runs(BATCHES[q]):
                    last = copy(rows_t[:, c, :, :, f:f + n].rearrange("d g s f -> d f s g"),
                                ps_t[b % 2][:, i:i + n, :].rearrange("d f (s g) -> d f s g", s=NS))
                last.then_inc(rows_t_copied, 1)

            act.wait_ge(ids_transposed, 1)
            copy(ids_t[:], ps_t[0][0:NT, :, :].rearrange("t c p -> t (c p)")).then_inc(ids_t_ready, 1)
            act.wait_ge(first_row_ready, 1)
            subtract_first_row(0)
            subtract_first_row(1)
            split_hi(1)
            act.wait_ge(dense_transposed, 1)
            copy(dense_t[:], ps_dve[0:ND, :, :]).then_inc(dense_copied, 1)
            for t in range(NT):
                if t + 2 < NT:
                    subtract_first_row(t + 2)
                    split_hi(t + 2)
                copy_looked_up(t)
                if t >= 1:
                    copy_rows_t(t - 1)

            def dots_step(c, j):
                if c > 0 and j == 0:
                    act.wait_ge(sym_blocks, c)
                if (c, j) == (0, 0):
                    act.wait_ge(dots_cleared, 1)
                act.wait_ge(products_done, NSTEP * c + j + 1)
                for s in range(0, NS // 2):
                    last = copy_dots(copy, c, j, s)
                last.then_inc(dots_by_act, 1)

            for b in range(NT - 1, 2 * NB - 1):
                copy_rows_t(b)
            dots_step(0, 0)
            dots_step(0, 1)
            copy_rows_t(2 * NB - 1)
            dots_step(0, 2)
            dots_step(0, 3)
            dots_step(1, 0)
            dots_step(1, 1)
            copy_z(0)
            dots_step(1, 2)
            relu1(0)
            copy_rows_t(2 * NB)
            dots_step(1, 3)
            copy_rows_t(2 * NB + 1)
            copy_rows_t(2 * NB + 2)
            relu2(0)
            copy_rows_t(2 * NB + 3)
            copy_y(0)
            copy_rows_t(2 * NB + 4)
            copy_z(1)
            dots_step(2, 0)
            copy_rows_t(3 * NB)
            dots_step(2, 1)
            relu1(1)
            dots_step(2, 2)
            copy_rows_t(3 * NB + 1)
            dots_step(2, 3)
            copy_rows_t(3 * NB + 2)
            relu2(1)
            relu2_second(1)
            copy_rows_t(3 * NB + 3)
            copy_z(2)
            copy_rows_t(3 * NB + 4)
            copy_y(1)
            relu1(2)
            for j in range(NSTEP):
                dots_step(3, j)
            relu1_second(2)
            act.wait_ge(sym_blocks, CH)
            repeat_columns(copy).then_inc(columns_repeated, 1)
            copy_z(3)
            relu1(3)
            relu2(2)
            relu2(3)
            copy_y(2)
            copy_y(3)

        @block.vector
        def _(dve):
            copy = nc.vector.tensor_copy

            def copy_z(c):
                dve.wait_ge(z_transposed, 2 * c + 2)
                copy(z_t[0:NP, c, 1:KC, :], ps_z(c)[1]).then_inc(z_rest, 1)

            def relu1(c):
                if c == 0:
                    dve.wait_ge(biases_loaded, 32)
                dve.wait_ge(layer1_done, O1 * (c + 1))
                for k in range(O1 // 2, O1):
                    last = nc.vector.tensor_scalar(h1[:, c % 2, k, :], ps_h(c, k, O1), b1_sb[:, k:k + 1], 0.0,
                                                   ALU.add, ALU.max)
                last.then_inc(h1_second, 1)

            def relu2(c):
                dve.wait_ge(layer2_done, 2 * c + 2)
                for k in range(O2 // 2, O2):
                    last = nc.vector.tensor_scalar(h2[:, c % 2, k, :], ps_h(c, k, O2), b2_sb[:, k:k + 1], 0.0,
                                                   ALU.add, ALU.max)
                last.then_inc(h2_second, 1)

            nc.vector.memset(nothing[:], 0.0).then_inc(nothing_ready, 1)
            nc.vector.memset(pads[:, 0:CH // 2], 0.0).then_inc(pads_ready, 1)
            dve.wait_ge(ident_ready, 1)
            copy(pick[:], ident[0:NT, 0:NT]).then_inc(pick_ready, 1)
            dve.wait_ge(ids_loaded, 16)
            for i, f, n in runs(ONE_HOT):
                last = copy(ids_f[:, :, i:i + n], ids_sb[:, :, f:f + n])
            last.then_inc(ids_converted, 1)
            nc.vector.memset(dots[:], 0.0).then_inc(dots_cleared, 1)
            dve.wait_ge(table_loaded[0], 32)
            copy(table_hi[0][:], table[0][:]).then_inc(first_hi_ready, 1)
            for t in range(NT):
                wait_for_hi(dve, t)
                dve.wait_ge(table_loaded[t % 3], 32 * (t // 3 + 1))
                if t >= 2:
                    dve.wait_ge(one_hot_used, KT * (t - 1))
                nc.vector.tensor_tensor(table_lo[t % 2][:], table[t % 3][:], table_hi[t % 3][:].bitcast(fp32),
                                        ALU.subtract).then_inc(lo_ready, 1)
                dve.wait_ge(id_less_row_ready, t + 1)
                for k in range(KT):
                    i = KT * t + k
                    if i >= RING:
                        dve.wait_ge(one_hot_used, i - RING + 1)
                    nc.vector.tensor_scalar(one_hot[:, i % RING, :], id_less_row[:, t, :], float(k), None,
                                            ALU.is_equal).then_inc(one_hot_ready, 1)

            def dots_step(c, j):
                if (c, j) == (0, 0):
                    dve.wait_ge(dots_cleared, 1)
                dve.wait_ge(products_done, NSTEP * c + j + 1)
                for s in range(NS // 2, NS):
                    last = copy_dots(copy, c, j, s)
                last.then_inc(dots_by_dve, 1)

            def pick_pairs(c):
                dve.wait_ge(dots_by_dve, NSTEP * (c + 1))
                dve.wait_ge(dots_by_act, NSTEP * (c + 1))
                nc.vector.transpose(sym[:].rearrange("p n m -> p m n")[:, 0:NF, :],
                                    dots[:]).then_inc(sym_blocks, 1)
                dve.wait_ge(sym_blocks, c + 1)
                if c > 0:
                    dve.wait_ge(z_transposed, 2 * c)
                if c < CH - 1:
                    repeat_columns(copy).then_inc(columns_repeated, 1)
                copy(pairs[:, 0:NF - NK, :], sym_pairs[:, 0:NF - NK, :])
                dve.wait_ge(columns_repeated, c + 1)
                copy(pairs[:, NF - NK:NF, :], sym_pairs[:, NF - NK:NF, :]).then_inc(pairs_ready, 1)

            for j in range(NSTEP):
                dots_step(0, j)
            pick_pairs(0)
            dots_step(1, 0)
            dots_step(1, 1)
            copy_z(0)
            dots_step(1, 2)
            relu1(0)
            dots_step(1, 3)
            pick_pairs(1)
            relu2(0)
            copy_z(1)
            dots_step(2, 0)
            dots_step(2, 1)
            dots_step(2, 2)
            relu1(1)
            dots_step(2, 3)
            pick_pairs(2)
            copy_z(2)
            for j in range(NSTEP):
                dots_step(3, j)
            pick_pairs(3)
            copy_z(3)
            relu1(3)
            relu2(2)
            relu2(3)

        @block.tensor
        def _(pe):
            def spread_ids(t):
                if t >= 2:
                    pe.wait_ge(id_less_row_ready, t - 1)
                nc.tensor.matmul(ps_ids[t % 2].rearrange("p c b -> p (c b)"),
                                 pick[:, t:t + 1].to_broadcast([NT, P]), ids_t[:],
                                 start=True, stop=True).then_inc(ids_spread, 1)

            def look_up(t):
                wait_for_hi(pe, t)
                pe.wait_ge(lo_ready, t + 1)
                if t >= 2:
                    pe.wait_ge(looked_up_copied, t - 1)
                bank = ps_rows[t % 2].rearrange("d c b -> d (c b)")
                for k in range(KT):
                    i = KT * t + k
                    pe.wait_ge(one_hot_ready, i + 1)
                    nc.tensor.matmul(bank, table_hi[t % 3][:, k, :], one_hot[:, i % RING, :],
                                     start=(k == 0), stop=False)
                    last = nc.tensor.matmul(bank, table_lo[t % 2][:, k, :], one_hot[:, i % RING, :],
                                            start=False, stop=(k == KT - 1))
                    last.then_inc(one_hot_used, 1)

            def transpose_rows(b):
                c, q = divmod(b, NB)
                pe.wait_ge(gathered[c % 2][q], 16 * len(BATCHES[q]) * (c // 2 + 1))
                if b >= 2:
                    pe.wait_ge(rows_t_copied, b - 1)
                for i in range(len(BATCHES[q])):
                    last = nc.tensor.transpose(ps_t[b % 2][:, i, :], rows[c % 2][:, QF * q + i, :], ident[:])
                last.then_inc(rows_transposed, 1)

            def multiply_rows(c, j):
                if j == 0:
                    pe.wait_ge(rows_t_copied, NB * (c + 1))
                    if c == 0:
                        pe.wait_ge(looked_up_copied, NT)
                        pe.wait_ge(pads_ready, 2)
                t = NSTEP * c + j
                if t >= 2:
                    pe.wait_ge(dots_by_act, t - 1)
                    pe.wait_ge(dots_by_dve, t - 1)
                for i in range(STEP):
                    g = STEP * j + i
                    last = nc.tensor.matmul(ps_g[t % 2][0:LIVE, i, 0:NS * NF],
                                            rows_t[:, c, g, :, :].rearrange("d s f -> d (s f)")[:, 0:LIVE],
                                            rows_t[:, c, g, :, 0:NF], start=True, stop=True)
                last.then_inc(products_done, 1)

            def transpose_pairs(c):
                pe.wait_ge(pairs_ready, c + 1)
                if 0 < c < CH - 1:
                    pe.wait_ge(h2_first, c)
                    pe.wait_ge(h2_second, c)
                    pe.wait_ge(y_copied, 1)
                for bank, ks in zip(ps_z(c), Z_CHUNKS):
                    for j, k in enumerate(ks):
                        chunk_pairs = pairs[:, NR * k:NR * (k + 1), :].rearrange("p n k -> p (n k)")
                        last = nc.tensor.transpose(bank[:, j, :], chunk_pairs, ident[:])
                    last.then_inc(z_transposed, 1)

            def layer1(c, o):
                if (c, o) == (0, 0):
                    pe.wait_ge(dense_copied, 1)
                    pe.wait_ge(dense_placed, 32)
                    pe.wait_ge(w1_loaded, 16 * len(W1_PIECES))
                for k in range(KC):
                    if o == 0 and k == 0:
                        pe.wait_ge(z_first, c + 1)
                    if o == 0 and k == 1:
                        pe.wait_ge(z_rest, c + 1)
                    K = KROWS[k]
                    last = nc.tensor.matmul(ps_h(c, o, O1), w1_sb[0:K, k, o:H1:O1], z_t[0:K, c, k, :],
                                            start=(k == 0), stop=(k == KC - 1))
                last.then_inc(layer1_done, 1)

            def layer2(c, o):
                if c == 0:
                    pe.wait_ge(w23_loaded, 32)
                pe.wait_ge(h1_first, c + 1)
                for k in range(O1):
                    if k == O1 // 2:
                        pe.wait_ge(h1_second, c + 1)
                    last = nc.tensor.matmul(ps_h(c, o, O2), w2_sb[:, k, o:H2:O2], h1[:, c % 2, k, :],
                                            start=(k == 0), stop=(k == O1 - 1))
                last.then_inc(layer2_done, 1)

            def layer3(c):
                for k in range(O2):
                    pe.wait_ge(h2_second if k else h2_first, c + 1)
                    last = nc.tensor.matmul(ps_y(c), h2[:, c % 2, k, :], w3_sb[:, k:k + 1],
                                            start=(k == 0), stop=(k == O2 - 1))
                last.then_inc(layer3_done, 1)

            def keep_busy(count):
                for _ in range(count):
                    nc.tensor.matmul(ps_g[0][:, 0:4, :].rearrange("p c b -> p (c b)"),
                                     nothing[:, 0:P], nothing[:], start=True, stop=True)

            pe.wait_ge(ident_ready, 1)
            pe.wait_ge(nothing_ready, 1)
            keep_busy(WARM[0])
            pe.wait_ge(ids_converted, 1)
            for c in range(CH):
                last = nc.tensor.transpose(ps_t[0][0:NT, c, :], ids_f[:, c, :], ident[:])
            last.then_inc(ids_transposed, 1)
            keep_busy(WARM[1])
            pe.wait_ge(ids_t_ready, 1)
            pe.wait_ge(pick_ready, 1)
            spread_ids(0)
            spread_ids(1)
            pe.wait_ge(dense_loaded, 16)
            for c in range(CH):
                last = nc.tensor.transpose(ps_dve[0:ND, c, :], dense_sb[:, c, :], ident[:])
            last.then_inc(dense_transposed, 1)
            for t in range(NT):
                look_up(t)
                if t + 2 < NT:
                    spread_ids(t + 2)
                if t >= 1:
                    transpose_rows(t - 1)
            for b in range(NT - 1, 2 * NB - 1):
                transpose_rows(b)
            multiply_rows(0, 0)
            multiply_rows(0, 1)
            transpose_rows(2 * NB - 1)
            multiply_rows(0, 2)
            multiply_rows(0, 3)
            multiply_rows(1, 0)
            multiply_rows(1, 1)
            transpose_pairs(0)
            multiply_rows(1, 2)
            layer1(0, 0)
            layer1(0, 1)
            transpose_rows(2 * NB)
            layer1(0, 2)
            layer1(0, 3)
            multiply_rows(1, 3)
            transpose_rows(2 * NB + 1)
            transpose_rows(2 * NB + 2)
            layer2(0, 0)
            layer2(0, 1)
            transpose_rows(2 * NB + 3)
            layer3(0)
            transpose_rows(2 * NB + 4)
            transpose_pairs(1)
            multiply_rows(2, 0)
            transpose_rows(3 * NB)
            multiply_rows(2, 1)
            layer1(1, 0)
            layer1(1, 1)
            multiply_rows(2, 2)
            layer1(1, 2)
            layer1(1, 3)
            transpose_rows(3 * NB + 1)
            multiply_rows(2, 3)
            transpose_rows(3 * NB + 2)
            layer2(1, 0)
            layer2(1, 1)
            transpose_rows(3 * NB + 3)
            transpose_pairs(2)
            layer1(2, 0)
            transpose_rows(3 * NB + 4)
            layer1(2, 1)
            layer3(1)
            for j in range(NSTEP):
                multiply_rows(3, j)
            layer1(2, 2)
            layer1(2, 3)
            layer2(2, 0)
            transpose_pairs(3)
            layer1(3, 0)
            layer1(3, 1)
            layer1(3, 2)
            layer1(3, 3)
            layer2(2, 1)
            layer2(3, 0)
            layer2(3, 1)
            layer3(2)
            layer3(3)


def kernel(**inputs):
    import numpy as np
    import concourse.bacc as bacc
    from concourse.bass_utils import run_bass_kernel_spmd

    nc = bacc.Bacc("TRN2", target_bir_lowering=False, num_devices=1)
    arrays, aps = {}, {}
    for name, value in inputs.items():
        a = np.ascontiguousarray(value)
        arrays[f"in_{name}"] = a.view(np.uint32) if name == "ids" else a
        aps[name] = nc.dram_tensor(f"in_{name}", a.shape, mybir.dt.from_np(arrays[f"in_{name}"].dtype),
                                   kind="ExternalInput").ap()
    out = nc.dram_tensor("out", (inputs["dense_ctx"].shape[0], 1), mybir.dt.float32, kind="ExternalOutput").ap()
    dlrm_tower(nc, aps["dense_ctx"], aps["ids"], [aps[f"tbl_{f}"] for f in range(NF)],
               aps["W_top1"], aps["b_top1"], aps["W_top2"], aps["b_top2"], aps["W_top3"], out)
    return run_bass_kernel_spmd(nc, [arrays], core_ids=[0]).results[0]["out"]
```
